# Optimizing a Trainium2 kernel written in Bass

```python
import numpy as np
import jax
import jax.numpy as jnp

def _softmax(x, axis=-1):
    return jax.nn.softmax(x, axis=axis)

def _gelu(x):
    return jax.nn.gelu(x, approximate=True)

def _silu(x):
    return jax.nn.silu(x)

def _sigmoid(x):
    return jax.nn.sigmoid(x)

def _layernorm(x, axis=-1, eps=1e-05):
    m = jnp.mean(x, axis=axis, keepdims=True)
    v = jnp.var(x, axis=axis, keepdims=True)
    return (x - m) / jnp.sqrt(v + eps)

def _scatter_add(tgt, idx, src, axis=0):
    return tgt.at[idx].add(src)

def _segment_sum(src, seg, n):
    return jax.ops.segment_sum(src, seg, n)
kernel_name = 'mk_adaln_attn_ffn_d1_seqx_r8_7dfd1f'

def setup_inputs(seed: int=0):
    np.random.seed(seed)
    _w = jnp.asarray

    def _rec_inputs():
        import jax
        import jax.numpy as jnp
        _rk = jax.random.key(seed)
        x = 7.22e-05 + 1 * jax.random.normal(jax.random.fold_in(_rk, 1), (32, 32, 128), jnp.float32)
        _lenS = 32 - jax.random.randint(jax.random.fold_in(_rk, 7), (32,), 0, max(1, 32 // 4) + 1, jnp.int32)
        _lenS2 = 32 - jax.random.randint(jax.random.fold_in(_rk, 8), (32,), 0, max(1, 32 // 4) + 1, jnp.int32)
        cond_64 = -0.104238 + 1.01173 * jax.random.normal(jax.random.fold_in(_rk, 11), (32, 64), jnp.float32)
        _validS = jnp.arange(32)[None, :] < _lenS[:, None]
        _validS2 = jnp.arange(32)[None, :] < _lenS2[:, None]
        _causal = jnp.tril(jnp.ones((32, 32), dtype=bool))
        mask_BxS_bf1 = jnp.ones((32, 32), dtype=bool)
        return (x, cond_64, mask_BxS_bf1)
    x, cond_64, mask_BxS_bf1 = _rec_inputs()

    def _L0_cond_setup():
        import jax, jax.numpy as jnp
        import numpy as np
        B, S, H = (4, 256, 128)
        E = 8
        M = 64
        K = 2
        N_SHARED = 2
        SM = M * N_SHARED
        G = 64
        GE_TEMP = 1.0
        ALPHA = 0.001
        SEQ_AUX = True
        NORM_TOPK = True
        COS_TEMP = 0.78
        CONS_ALPHA = 0.01
        LEAKY_SLOPE = 0.01
        EPS_COS = 1e-08

        def _leaky(x):
            return jnp.where(x >= 0, x, LEAKY_SLOPE * x)

        def _moe_forward(hidden_states, g, wt, wg, w_gate, w_up, w_down, sw_gate, sw_up, sw_down):
            b, s, h = hidden_states.shape
            x = hidden_states.reshape(-1, h)
            T = x.shape[0]
            logits_h = x @ wt.T
            logits_g = g @ wg.T
            logits_g = jnp.repeat(logits_g, s, axis=0)
            logits = (logits_h + logits_g / GE_TEMP) / (1.0 + 1.0 / GE_TEMP)
            scores = jax.nn.softmax(logits, axis=-1)
            topk_w, topk_idx = jax.lax.top_k(scores, K)
            if K > 1 and NORM_TOPK:
                topk_w = topk_w / (topk_w.sum(-1, keepdims=True) + 1e-20)
            onehot = jax.nn.one_hot(topk_idx.reshape(b, s * K), E, dtype=jnp.float32)
            ce = onehot.sum(1) / (s * K / E)
            aux_loss = (ce * scores.reshape(b, s, E).mean(1)).sum(1).mean() * ALPHA
            gp = _leaky(jnp.einsum('th,ehm->etm', x, w_gate))
            up = jnp.einsum('th,ehm->etm', x, w_up)
            y_all = jnp.einsum('etm,emh->eth', gp * up, w_down)
            y_sel = y_all[topk_idx, jnp.arange(T)[:, None], :]
            y = (y_sel * topk_w[..., None]).sum(1).reshape(b, s, h)
            p = _leaky(hidden_states @ sw_gate) * (hidden_states @ sw_up) @ sw_down
            y = y + p
            num = jnp.sum(y * p, -1)
            den = jnp.maximum(jnp.linalg.norm(y, axis=-1), EPS_COS) * jnp.maximum(jnp.linalg.norm(p, axis=-1), EPS_COS)
            closs = CONS_ALPHA * jnp.mean(num / den / (1.0 + COS_TEMP))
            return (y, aux_loss + closs)
        key = jax.random.key(seed)
        ks = jax.random.split(key, 12)
        sh = 1.0 / np.sqrt(H)
        sm = 1.0 / np.sqrt(M)
        ssm = 1.0 / np.sqrt(SM)
        sg = 1.0 / np.sqrt(G)
        return {'hidden_states': jax.random.normal(ks[0], (B, S, H), jnp.float32), 'g': jax.random.normal(ks[1], (B, G), jnp.float32), 'wt': jax.random.uniform(ks[2], (E, H), jnp.float32, -sh, sh), 'wg': jax.random.uniform(ks[3], (E, G), jnp.float32, -sg, sg), 'w_gate': jax.random.uniform(ks[4], (E, H, M), jnp.float32, -sh, sh), 'w_up': jax.random.uniform(ks[5], (E, H, M), jnp.float32, -sh, sh), 'w_down': jax.random.uniform(ks[6], (E, M, H), jnp.float32, -sm, sm), 'sw_gate': jax.random.uniform(ks[7], (H, SM), jnp.float32, -sh, sh), 'sw_up': jax.random.uniform(ks[8], (H, SM), jnp.float32, -sh, sh), 'sw_down': jax.random.uniform(ks[9], (SM, H), jnp.float32, -ssm, ssm)}
    _L0_cond_all = _L0_cond_setup()
    _L0_cond_in = {k: v for k, v in _L0_cond_all.items() if k in ('wt', 'wg', 'w_gate', 'w_up', 'w_down', 'sw_gate', 'sw_up', 'sw_down')}
    del _L0_cond_all

    def _L0_attn_setup():
        import jax, jax.numpy as jnp
        import numpy as np
        B, T, D, H = (2, 256, 128, 16)
        HD = D // H
        SCALE = HD ** (-0.5)
        key = jax.random.key(seed)
        k1, k2, k3 = jax.random.split(key, 3)
        x = jax.random.normal(k1, (B, T, D), dtype=jnp.float32)
        w_qkv = jax.random.normal(k2, (D, 3 * D), dtype=jnp.float32) * D ** (-0.5)
        w_proj = jax.random.normal(k3, (D, D), dtype=jnp.float32) * D ** (-0.5)
        b_proj = jnp.zeros((D,), dtype=jnp.float32)
        return {'x': x, 'w_qkv': w_qkv, 'w_proj': w_proj, 'b_proj': b_proj}
    _L0_attn_all = _L0_attn_setup()
    _L0_attn_in = {k: v for k, v in _L0_attn_all.items() if k in ('w_qkv', 'w_proj', 'b_proj')}
    del _L0_attn_all

    def _L0_cond2_setup():
        import jax, jax.numpy as jnp
        import numpy as np
        DIM = 128
        HEADS = 16
        DIM_HEAD = 64
        SCALE = 8.0

        def ln(x, g, eps=1e-05):
            mean = x.mean(axis=-1, keepdims=True)
            var = ((x - mean) ** 2).mean(axis=-1, keepdims=True)
            return (x - mean) * jax.lax.rsqrt(var + eps) * g

        def l2norm(t):
            n = jnp.maximum(jnp.linalg.norm(t, axis=-1, keepdims=True), 1e-12)
            return t / n

        def rel_pos_bias(n, w0, b0, g0, w1, b1, g1, w2, b2, dtype):
            pos = jnp.arange(-n + 1, n, dtype=dtype)[:, None]
            h = jax.nn.silu(ln(pos @ w0 + b0, g0))
            h = jax.nn.silu(ln(h @ w1 + b1, g1))
            h = h @ w2 + b2
            i = jnp.arange(n)
            idx = i[:, None] - i[None, :] + n - 1
            bias = h[idx]
            return jnp.transpose(bias, (2, 0, 1))
        key = jax.random.key(seed)
        ks = jax.random.split(key, 16)
        b, n = (2, 256)
        inner = HEADS * DIM_HEAD
        s = 0.02
        return {'x': jax.random.normal(ks[0], (b, n, DIM), jnp.float32), 'mask': jnp.ones((b, n), dtype=bool), 'g_norm': jnp.ones((DIM,), jnp.float32), 'Wq': jax.random.normal(ks[1], (DIM, inner), jnp.float32) * s, 'Wkv': jax.random.normal(ks[2], (DIM, 2 * DIM_HEAD), jnp.float32) * s, 'q_scale': jnp.ones((DIM_HEAD,), jnp.float32), 'k_scale': jnp.ones((DIM_HEAD,), jnp.float32), 'null_kv': jax.random.normal(ks[3], (2, DIM_HEAD), jnp.float32), 'null_attn_bias': jax.random.normal(ks[4], (HEADS,), jnp.float32), 'w0': jax.random.normal(ks[5], (1, DIM), jnp.float32) * s, 'b0': jnp.zeros((DIM,), jnp.float32), 'g0': jnp.ones((DIM,), jnp.float32), 'w1': jax.random.normal(ks[6], (DIM, DIM), jnp.float32) * s, 'b1': jnp.zeros((DIM,), jnp.float32), 'g1': jnp.ones((DIM,), jnp.float32), 'w2': jax.random.normal(ks[7], (DIM, HEADS), jnp.float32) * s, 'b2': jnp.zeros((HEADS,), jnp.float32), 'Wout': jax.random.normal(ks[8], (inner, DIM), jnp.float32) * s, 'g_out': jnp.ones((DIM,), jnp.float32)}
    _L0_cond2_all = _L0_cond2_setup()
    _L0_cond2_in = {k: v for k, v in _L0_cond2_all.items() if k in ('g_norm', 'Wq', 'Wkv', 'q_scale', 'k_scale', 'null_attn_bias', 'w0', 'b0', 'g0', 'w1', 'b1', 'g1', 'w2', 'b2', 'Wout', 'g_out')}
    del _L0_cond2_all

    def _L0_ffn_setup():
        import jax, jax.numpy as jnp
        import numpy as np
        EPS = 1e-09
        RMS_EPS = 1e-06
        TOP_K = 2
        LOOPS = 2

        def _rmsnorm(x, w):
            var = jnp.mean(x * x, axis=-1, keepdims=True)
            return x * jax.lax.rsqrt(var + RMS_EPS) * w

        def _swiglu(x, w1, w3, w2):
            h = jax.nn.silu(x @ w1) * (x @ w3)
            return h @ w2
        key = jax.random.key(seed)
        ks = jax.random.split(key, 5)
        B, S, D, F, E = (4, 256, 128, 256, 8)
        z = jax.random.normal(ks[0], (B, S, D), dtype=jnp.float32)
        norm_w = jnp.ones((D,), dtype=jnp.float32)
        router_w = jax.random.normal(ks[1], (D, E), dtype=jnp.float32) * 0.02
        w1 = jax.random.normal(ks[2], (E, D, F), dtype=jnp.float32) * 0.02
        w3 = jax.random.normal(ks[3], (E, D, F), dtype=jnp.float32) * 0.02
        w2 = jax.random.normal(ks[4], (E, F, D), dtype=jnp.float32) * 0.02
        return {'z': z, 'norm_w': norm_w, 'router_w': router_w, 'w1': w1, 'w3': w3, 'w2': w2}
    _L0_ffn_all = _L0_ffn_setup()
    _L0_ffn_in = {k: v for k, v in _L0_ffn_all.items() if k in ('norm_w', 'router_w', 'w1', 'w3', 'w2')}
    del _L0_ffn_all
    return {'x': x, 'cond_64': cond_64, 'mask_BxS_bf1': mask_BxS_bf1, 'L0_cond_wt': _L0_cond_in['wt'], 'L0_cond_wg': _L0_cond_in['wg'], 'L0_cond_w_gate': _L0_cond_in['w_gate'], 'L0_cond_w_up': _L0_cond_in['w_up'], 'L0_cond_w_down': _L0_cond_in['w_down'], 'L0_cond_sw_gate': _L0_cond_in['sw_gate'], 'L0_cond_sw_up': _L0_cond_in['sw_up'], 'L0_cond_sw_down': _L0_cond_in['sw_down'], 'L0_attn_w_qkv': _L0_attn_in['w_qkv'], 'L0_attn_w_proj': _L0_attn_in['w_proj'], 'L0_attn_b_proj': _L0_attn_in['b_proj'], 'L0_cond2_g_norm': _L0_cond2_in['g_norm'], 'L0_cond2_Wq': _L0_cond2_in['Wq'], 'L0_cond2_Wkv': _L0_cond2_in['Wkv'], 'L0_cond2_q_scale': _L0_cond2_in['q_scale'], 'L0_cond2_k_scale': _L0_cond2_in['k_scale'], 'L0_cond2_null_attn_bias': _L0_cond2_in['null_attn_bias'], 'L0_cond2_w0': _L0_cond2_in['w0'], 'L0_cond2_b0': _L0_cond2_in['b0'], 'L0_cond2_g0': _L0_cond2_in['g0'], 'L0_cond2_w1': _L0_cond2_in['w1'], 'L0_cond2_b1': _L0_cond2_in['b1'], 'L0_cond2_g1': _L0_cond2_in['g1'], 'L0_cond2_w2': _L0_cond2_in['w2'], 'L0_cond2_b2': _L0_cond2_in['b2'], 'L0_cond2_Wout': _L0_cond2_in['Wout'], 'L0_cond2_g_out': _L0_cond2_in['g_out'], 'L0_ffn_norm_w': _L0_ffn_in['norm_w'], 'L0_ffn_router_w': _L0_ffn_in['router_w'], 'L0_ffn_w1': _L0_ffn_in['w1'], 'L0_ffn_w3': _L0_ffn_in['w3'], 'L0_ffn_w2': _L0_ffn_in['w2']}

def reference(x, cond_64, mask_BxS_bf1, L0_cond_wt, L0_cond_wg, L0_cond_w_gate, L0_cond_w_up, L0_cond_w_down, L0_cond_sw_gate, L0_cond_sw_up, L0_cond_sw_down, L0_attn_w_qkv, L0_attn_w_proj, L0_attn_b_proj, L0_cond2_g_norm, L0_cond2_Wq, L0_cond2_Wkv, L0_cond2_q_scale, L0_cond2_k_scale, L0_cond2_null_attn_bias, L0_cond2_w0, L0_cond2_b0, L0_cond2_g0, L0_cond2_w1, L0_cond2_b1, L0_cond2_g1, L0_cond2_w2, L0_cond2_b2, L0_cond2_Wout, L0_cond2_g_out, L0_ffn_norm_w, L0_ffn_router_w, L0_ffn_w1, L0_ffn_w3, L0_ffn_w2):
    import jax
    import jax.numpy as jnp

    def _L0_cond_ref(hidden_states, g, wt, wg, w_gate, w_up, w_down, sw_gate, sw_up, sw_down):
        import jax, jax.numpy as jnp
        import numpy as np
        B, S, H = (4, 256, 128)
        E = 8
        M = 64
        K = 2
        N_SHARED = 2
        SM = M * N_SHARED
        G = 64
        GE_TEMP = 1.0
        ALPHA = 0.001
        SEQ_AUX = True
        NORM_TOPK = True
        COS_TEMP = 0.78
        CONS_ALPHA = 0.01
        LEAKY_SLOPE = 0.01
        EPS_COS = 1e-08

        def _leaky(x):
            return jnp.where(x >= 0, x, LEAKY_SLOPE * x)

        def _moe_forward(hidden_states, g, wt, wg, w_gate, w_up, w_down, sw_gate, sw_up, sw_down):
            b, s, h = hidden_states.shape
            x = hidden_states.reshape(-1, h)
            T = x.shape[0]
            logits_h = x @ wt.T
            logits_g = g @ wg.T
            logits_g = jnp.repeat(logits_g, s, axis=0)
            logits = (logits_h + logits_g / GE_TEMP) / (1.0 + 1.0 / GE_TEMP)
            scores = jax.nn.softmax(logits, axis=-1)
            topk_w, topk_idx = jax.lax.top_k(scores, K)
            if K > 1 and NORM_TOPK:
                topk_w = topk_w / (topk_w.sum(-1, keepdims=True) + 1e-20)
            onehot = jax.nn.one_hot(topk_idx.reshape(b, s * K), E, dtype=jnp.float32)
            ce = onehot.sum(1) / (s * K / E)
            aux_loss = (ce * scores.reshape(b, s, E).mean(1)).sum(1).mean() * ALPHA
            gp = _leaky(jnp.einsum('th,ehm->etm', x, w_gate))
            up = jnp.einsum('th,ehm->etm', x, w_up)
            y_all = jnp.einsum('etm,emh->eth', gp * up, w_down)
            y_sel = y_all[topk_idx, jnp.arange(T)[:, None], :]
            y = (y_sel * topk_w[..., None]).sum(1).reshape(b, s, h)
            p = _leaky(hidden_states @ sw_gate) * (hidden_states @ sw_up) @ sw_down
            y = y + p
            num = jnp.sum(y * p, -1)
            den = jnp.maximum(jnp.linalg.norm(y, axis=-1), EPS_COS) * jnp.maximum(jnp.linalg.norm(p, axis=-1), EPS_COS)
            closs = CONS_ALPHA * jnp.mean(num / den / (1.0 + COS_TEMP))
            return (y, aux_loss + closs)
        y, _ = _moe_forward(hidden_states, g, wt, wg, w_gate, w_up, w_down, sw_gate, sw_up, sw_down)
        return y

    def _L0_attn_ref(x, w_qkv, w_proj, b_proj):
        import jax, jax.numpy as jnp
        import numpy as np
        B, T, D, H = (2, 256, 128, 16)
        HD = D // H
        SCALE = HD ** (-0.5)
        b, t, d = x.shape
        qkv = jnp.einsum('btd,de->bte', x, w_qkv)
        qkv = qkv.reshape(b, t, 3, H, HD)
        q = qkv[:, :, 0].transpose(0, 2, 1, 3)
        k = qkv[:, :, 1].transpose(0, 2, 1, 3)
        v = qkv[:, :, 2].transpose(0, 2, 1, 3)
        scores = jnp.einsum('bhqd,bhkd->bhqk', q, k) * SCALE
        probs = jax.nn.softmax(scores, axis=1)
        attn_out = jnp.einsum('bhqk,bhkd->bhqd', probs, v)
        attn_out = attn_out.transpose(0, 2, 1, 3).reshape(b, t, d)
        out = jnp.einsum('btd,de->bte', attn_out, w_proj) + b_proj
        return out

    def _L0_cond2_ref(x, mask, g_norm, Wq, Wkv, q_scale, k_scale, null_kv, null_attn_bias, w0, b0, g0, w1, b1, g1, w2, b2, Wout, g_out):
        import jax, jax.numpy as jnp
        import numpy as np
        DIM = 128
        HEADS = 16
        DIM_HEAD = 64
        SCALE = 8.0

        def ln(x, g, eps=1e-05):
            mean = x.mean(axis=-1, keepdims=True)
            var = ((x - mean) ** 2).mean(axis=-1, keepdims=True)
            return (x - mean) * jax.lax.rsqrt(var + eps) * g

        def l2norm(t):
            n = jnp.maximum(jnp.linalg.norm(t, axis=-1, keepdims=True), 1e-12)
            return t / n

        def rel_pos_bias(n, w0, b0, g0, w1, b1, g1, w2, b2, dtype):
            pos = jnp.arange(-n + 1, n, dtype=dtype)[:, None]
            h = jax.nn.silu(ln(pos @ w0 + b0, g0))
            h = jax.nn.silu(ln(h @ w1 + b1, g1))
            h = h @ w2 + b2
            i = jnp.arange(n)
            idx = i[:, None] - i[None, :] + n - 1
            bias = h[idx]
            return jnp.transpose(bias, (2, 0, 1))
        b, n, _ = x.shape
        xn = ln(x, g_norm)
        q = (xn @ Wq).reshape(b, n, HEADS, DIM_HEAD).transpose(0, 2, 1, 3)
        kv = xn @ Wkv
        k, v = (kv[..., :DIM_HEAD], kv[..., DIM_HEAD:])
        nk = jnp.broadcast_to(null_kv[0], (b, 1, DIM_HEAD))
        nv = jnp.broadcast_to(null_kv[1], (b, 1, DIM_HEAD))
        k = jnp.concatenate([nk, k], axis=1)
        v = jnp.concatenate([nv, v], axis=1)
        q = l2norm(q) * q_scale
        k = l2norm(k) * k_scale
        sim = jnp.einsum('bhid,bjd->bhij', q, k) * SCALE
        bias = rel_pos_bias(n, w0, b0, g0, w1, b1, g1, w2, b2, q.dtype)
        null_bias = jnp.broadcast_to(null_attn_bias[:, None, None], (HEADS, n, 1))
        attn_bias = jnp.concatenate([null_bias, bias], axis=-1)
        sim = sim + attn_bias
        neg = -jnp.finfo(sim.dtype).max
        causal = jnp.triu(jnp.ones((n, n + 1), dtype=bool), k=2)
        sim = jnp.where(causal, neg, sim)
        m = jnp.pad(mask, ((0, 0), (1, 0)), constant_values=True)[:, None, None, :]
        sim = jnp.where(m, sim, neg)
        attn = jax.nn.softmax(sim, axis=-1)
        out = jnp.einsum('bhij,bjd->bhid', attn, v)
        out = out.transpose(0, 2, 1, 3).reshape(b, n, HEADS * DIM_HEAD)
        return ln(out @ Wout, g_out)

    def _L0_ffn_ref(z, norm_w, router_w, w1, w3, w2):
        import jax, jax.numpy as jnp
        import numpy as np
        EPS = 1e-09
        RMS_EPS = 1e-06
        TOP_K = 2
        LOOPS = 2

        def _rmsnorm(x, w):
            var = jnp.mean(x * x, axis=-1, keepdims=True)
            return x * jax.lax.rsqrt(var + RMS_EPS) * w

        def _swiglu(x, w1, w3, w2):
            h = jax.nn.silu(x @ w1) * (x @ w3)
            return h @ w2
        B, S, D = z.shape
        E = router_w.shape[-1]
        T = B * S
        for _ in range(LOOPS):
            z_norm = _rmsnorm(z, norm_w)
            logits = z_norm @ router_w
            scores = jax.nn.softmax(logits, axis=-1)
            topk_vals, topk_idx = jax.lax.top_k(scores, TOP_K)
            topk_vals = topk_vals / (jnp.sum(topk_vals, axis=-1, keepdims=True) + EPS)
            cw = jnp.sum(jax.nn.one_hot(topk_idx, E, dtype=z.dtype) * topk_vals[..., None], axis=-2)
            flat_z = z_norm.reshape(T, D)
            flat_cw = cw.reshape(T, E)
            mixed = jnp.zeros((T, D), dtype=z.dtype)
            for e in range(E):
                mixed = mixed + flat_cw[:, e:e + 1] * _swiglu(flat_z, w1[e], w3[e], w2[e])
            z = z + mixed.reshape(B, S, D)
        return z
    x = x + _L0_attn_ref(_L0_cond_ref(x, cond_64, L0_cond_wt, L0_cond_wg, L0_cond_w_gate, L0_cond_w_up, L0_cond_w_down, L0_cond_sw_gate, L0_cond_sw_up, L0_cond_sw_down), L0_attn_w_qkv, L0_attn_w_proj, L0_attn_b_proj)
    x = x + _L0_ffn_ref(_L0_cond2_ref(x, mask_BxS_bf1, L0_cond2_g_norm, L0_cond2_Wq, L0_cond2_Wkv, L0_cond2_q_scale, L0_cond2_k_scale, cond_64, L0_cond2_null_attn_bias, L0_cond2_w0, L0_cond2_b0, L0_cond2_g0, L0_cond2_w1, L0_cond2_b1, L0_cond2_g1, L0_cond2_w2, L0_cond2_b2, L0_cond2_Wout, L0_cond2_g_out), L0_ffn_norm_w, L0_ffn_router_w, L0_ffn_w1, L0_ffn_w3, L0_ffn_w2)
    return x

_drawn_inputs = setup_inputs


def setup_inputs(seed=0):
    import zlib

    import numpy as np

    out = dict(_drawn_inputs(seed))
    spreads = {'L0_attn_b_proj': (0.0, 0.1),
     'L0_cond2_g_norm': (1.0, 0.2),
     'L0_cond2_q_scale': (1.0, 0.2),
     'L0_cond2_k_scale': (1.0, 0.2),
     'L0_cond2_b0': (0.0, 0.1),
     'L0_cond2_g0': (1.0, 0.6),
     'L0_cond2_b1': (0.0, 0.348),
     'L0_cond2_g1': (1.0, 0.6),
     'L0_cond2_b2': (0.0, 0.1),
     'L0_cond2_g_out': (1.0, 0.2),
     'L0_ffn_norm_w': (1.0, 0.6)}
    factors = {'L0_ffn_router_w': 6.894, 'L0_ffn_w1': 6.097, 'L0_ffn_w3': 5.914, 'L0_ffn_w2': 6.003}
    for name, (base, spread) in spreads.items():
        noise = np.random.default_rng([zlib.crc32(name.encode()), seed]).standard_normal(out[name].shape)
        drawn = base * np.exp(spread * noise) if base else spread * noise
        out[name] = jnp.asarray(drawn.astype(out[name].dtype))
    for name, factor in factors.items():
        out[name] = (out[name] * factor).astype(out[name].dtype)
    return out
```

```python
from contextlib import ExitStack

import numpy as np

import concourse.bass as bass
from concourse import mybir

F32 = mybir.dt.float32
F32R = mybir.dt.float32r
U8 = mybir.dt.uint8
ALU = mybir.AluOpType
ACT = mybir.ActivationFunctionType
AX_X = mybir.AxisListType.X

P = 128
SEQ = 32
NSEQ = 32
D = 128
TOK = SEQ * NSEQ
HALF = 512
NH = TOK // HALF
TILES = TOK // P
TPH = HALF // P
SPT = P // SEQ
SPH = HALF // SEQ
E = 8
M = 64
PAIRS = E // 2
UNITS = PAIRS + 1
G = 64
F = 256
FC = F // P
LOOPS = 2
AH, AD = 16, 8
AG = 4
CH, CD = 16, 64
HP = CH // 2
KEYS = SEQ + 1
KC = 2 * KEYS
HC = 4 * KC
BANKS = 8
SM_COLS = HP * KC
NEG = -1.0e30

COLS = ["g_norm", "norm_w", "q_scale", "k_scale", "null_k"]
ROWS = [("b_proj", D), ("g_out", D), ("null_bias", CH), ("w0", D), ("b0", D), ("g0", D),
        ("b1", D), ("g1", D), ("b2", CH)]


def offsets(parts):
    at, out = 0, {}
    for name, width in parts:
        out[name] = (at, at + width)
        at += width
    return out, at


CONST_AT, CONST_W = offsets([
    ("ident", P), ("mask_g", AG), ("mask_j", AG), ("mask_v", 4), ("mask_vc", 2), ("ones_pair", 2 * 32),
    ("ones_h2", P), ("causal", KEYS), ("rank", E), ("power", 16), ("position", 1), ("toeplitz", 64),
    ("select", PAIRS * P)])
WIDE_CONSTS = CONST_AT["position"][0]
PACK_A_AT, PACK_A_W = offsets([
    ("wt", E), ("s_gate", P), ("s_up", P), ("gate", PAIRS * P), ("up", PAIRS * P), ("down", PAIRS * D),
    ("s_down", D)])
PACK_B_AT, PACK_B_W = offsets([
    ("wqkv", 3 * D), ("wproj", D), ("cols", len(COLS)), ("wk", CD), ("wv", CD), ("router", E),
    ("rel_w1", D), ("rel_w2", CH)])
PACK_C_AT, PACK_C_W = offsets([("cond", NSEQ), ("wg", E)])
ROW_AT, ROW_W = offsets(ROWS)


def constants():
    c = np.zeros((P, CONST_W), np.float32)
    p = np.arange(P)

    def put(name, a):
        lo, hi = CONST_AT[name]
        c[:a.shape[0], lo:hi] = a.reshape(a.shape[0], hi - lo)

    put("ident", np.eye(P))
    put("mask_g", (p[:, None] // 32 == np.arange(AG)) * AD ** -0.5)
    put("mask_j", p[:, None] // AD % 4 == np.arange(4))
    put("mask_v", p[:, None] // 32 == np.arange(4))
    put("mask_vc", p[:, None] // 32 == np.arange(2))
    ones = np.zeros((P, 2, 32))
    for a in range(2):
        for h2 in range(2):
            ones[64 * h2:64 * h2 + 64, a, 2 * a + h2] = 1
    put("ones_pair", ones)
    put("ones_h2", p[:, None] // 64 == p // 64)
    put("toeplitz", (np.arange(64) - 31)[None, :] == np.arange(SEQ)[:, None])
    r = np.arange(16) % E
    put("select", np.concatenate([r[:, None] == 2 * u + p // M for u in range(PAIRS)], 1))
    q = p % SEQ
    put("causal", np.concatenate([(np.arange(SEQ) > q[:, None]) * NEG, np.zeros((P, 1))], 1))
    put("rank", np.tile(np.arange(E, 0, -1.0), (P, 1)))
    put("position", q[:, None])
    put("power", np.full((P, 16), -0.5))
    return c


def make_plan():
    def a_units(h):
        for u in (PAIRS, *range(PAIRS)):
            yield from (("ga", h, u), ("ua", h, u))

    def attention_b(h, after):
        if after is None:
            return [st for t in range(TPH) for st in
                    [("bs", h, t), ("bv", h, t)] + [("bn", h, t - 1)] * (t > 0)] + [("bn", h, TPH - 1)]
        second = b_second(after)
        out = []
        for t in range(TPH + 2):
            out += second[t]
            out += [("bv", h, t - 1)] * (1 <= t <= TPH) + [("bs", h, t)] * (t < TPH)
            out += [("bn", h, t - 1)] * (1 <= t <= TPH)
        return out + [st for part in second[TPH + 2:] for st in part]

    def b_second(h):
        out = []
        for t in range(TPH + 2):
            part = []
            if t < TPH:
                part.append(("bt", h, t))
            if 0 <= t - 1 < TPH:
                part.append(("bp", h, t - 1))
            if 0 <= t - 2 < TPH:
                part.append(("bo", h, t - 2))
            out.append(part)
        return out + [[("ln", h)]]

    def c_first(h):
        yield from (("ln2", h), ("xn", h), ("ck", h))
        for hp in range(HP):
            yield ("cq", h, hp)
        yield from (("ck2", h), ("kT", h), ("ss", h))
        for t in range(TPH):
            yield ("cv", h, t)
        yield ("s2", h)

    def c_second(h):
        out = []
        for t in range(TPH + 5):
            part = []
            if t < TPH:
                part += [("bm", h, t), ("cs", h, t, 0), ("cs", h, t, 1), ("ca", h, t)]
            if 0 <= t - 1 < TPH:
                part += [("cm", h, t - 1)]
            if 0 <= t - 2 < TPH:
                part += [("cn", h, t - 2)]
            if 0 <= t - 3 < TPH:
                part += [("ct", h, t - 3, 0), ("ct", h, t - 3, 1)]
            if 0 <= t - 4 < TPH:
                part += [("cp", h, t - 4, 0), ("cp", h, t - 4, 1)]
            if 0 <= t - 5 < TPH:
                part += [("co", h, t - 5)]
            out.append(part)
        return out

    def prepare(l, h):
        return [("fn", l, h), ("fm", l, h), ("fT", l, h), ("fr", l, h), ("fw", l, h)]

    def experts(l, h):
        out = []
        for e in range(E + 1):
            if e < E:
                for f in range(FC):
                    out += [("g", l, h, e, f), ("u", l, h, e, f)]
            if e:
                out += [("y", l, h, e - 1)]
        return out

    def flat(parts):
        return [st for part in parts for st in part]

    def merge(a, b):
        at = sorted([((i + 0.5) / len(a), 0, i) for i in range(len(a))] +
                    [((i + 0.5) / len(b), 1, i) for i in range(len(b))])
        return [(a, b)[which][i] for _, which, i in at]

    units = [list(a_units(h)) for h in range(NH)]
    plan = [("xT", 0), ("lg", 0), ("xT", 1), ("lg", 1), ("w", 0), *units[0], ("w", 1), ("wT", 0)]
    plan += [("wB", 0, u) for u in range(PAIRS)]
    plan += [*units[1][:4], ("yT", 0), *units[1][4:], ("wT", 1)]
    plan += [("wB", 1, u) for u in range(PAIRS)]
    start = attention_b(0, None)
    at = start.index(("bs", 0, TPH - 1)) + 1
    plan += [("bq", 0), ("bk", 0), ("yT", 1), *start[:at], ("bq", 1), ("bk", 1), *start[at:]]
    rel = [("rel1",), ("split_q", 0), ("relT1",), ("relM1",), ("split_q", 1), ("null",), ("relT2",),
           ("split", 0), ("relM2",), ("split", 1), ("bias", 0), ("split", 2), ("bias", 1)]
    plan += [rel[0]] + merge(attention_b(1, 0), rel[1:])
    splits = [("split", e) for e in range(3, E)]
    rest = flat(b_second(1))
    ahead = 7
    plan += merge([("ln2", 0), *rest[:ahead], ("xn", 0), ("ck", 0), *rest[ahead:]], splits)
    first = [list(c_first(h)) for h in range(NH)]
    second = [c_second(h) for h in range(NH)]
    plan += first[0][3:]
    plan += flat(second[0][:TPH])
    plan += merge(flat(second[0][TPH:]), first[1][:-TPH - 1])
    plan += merge(first[1][-TPH - 1:], prepare(0, 0))
    body = experts(0, 0)
    cut = len(body) * 5 // 8
    plan += merge(body[:cut], flat(second[1])) + merge(body[cut:], prepare(0, 1))
    for (l, h), after in (((0, 1), (1, 0)), ((1, 0), (1, 1)), ((1, 1), None)):
        body = experts(l, h)
        cut = len(body) // 2
        plan += body[:cut] + (merge(body[cut:], prepare(*after)) if after else body[cut:])
        if l == LOOPS - 1:
            plan.append(("out", h))
    return plan


PE_STEPS = {"xT", "lg", "ga", "ua", "wT", "wB", "yT", "relT1", "relM1", "relT2", "relM2", "bias", "null",
            "bq", "bk", "bv", "bs", "bt", "bp", "bo", "xn", "ck", "kT", "cv", "cq", "ss", "s2", "cs", "ct",
            "cp", "co", "fT", "fr", "g", "u", "y"}
PLAN = make_plan()
NUMBER = {s: n for n, s in enumerate(s for s in PLAN if s[0] in PE_STEPS)}


def layer_kernel(nc, x, pack_a, pack_b, pack_c, rows, null_v, key_mask, w_q, w_out, w13, w2, consts, out):
    with ExitStack() as ctx:
        def sb(name, shape, dt=F32):
            return ctx.enter_context(nc.sbuf_tensor(name, shape, dt))

        def sem(name):
            return ctx.enter_context(nc.semaphore(name))

        bank = [ctx.enter_context(nc.psum_tensor(f"bank{i}", [P, 512], F32)) for i in range(BANKS)]

        c_sb = sb("c_sb", [P, CONST_W])
        a_sb = sb("a_sb", [P, PACK_A_W])
        b_sb = sb("b_sb", [P, PACK_B_W])
        g_sb = sb("g_sb", [G, PACK_C_W])
        r_sb = sb("r_sb", [P, ROW_W])

        def const(name, parts=P):
            return c_sb[0:parts, CONST_AT[name][0]:CONST_AT[name][1]]

        def pack_a_at(name):
            return a_sb[:, PACK_A_AT[name][0]:PACK_A_AT[name][1]]

        def pack_b_at(name):
            return b_sb[:, PACK_B_AT[name][0]:PACK_B_AT[name][1]]

        def row(name, parts=P):
            return r_sb[0:parts, ROW_AT[name][0]:ROW_AT[name][1]]

        def column(name):
            n = PACK_B_AT["cols"][0] + COLS.index(name)
            return b_sb[:, n:n + 1]

        ident = const("ident")
        wt, wqkv, wproj = pack_a_at("wt"), pack_b_at("wqkv"), pack_b_at("wproj")
        gate = pack_a_at("gate").rearrange("p (u m) -> p u m", u=PAIRS)
        up = pack_a_at("up").rearrange("p (u m) -> p u m", u=PAIRS)
        down = pack_a_at("down").rearrange("p (u n) -> p u n", u=PAIRS)
        sel_r = sb("sel_r", [16, PAIRS * P], F32R)
        wqh = sb("wqh", [P, HP * P], F32R)
        wql = sb("wql", [P, HP * P], F32R)
        wout_sb = sb("wout_sb", [P, HP, D])
        w13h = sb("w13h", [P, E, 2 * F], F32R)
        w13l = sb("w13l", [P, E, 2 * F], F32R)
        w2_sb = sb("w2_sb", [P, E, FC, D])

        xb = sb("xb", [P, TILES, D])
        z = sb("z", [P, TILES, D])
        xyT = sb("xyT", [P, NH, HALF])
        nT = sb("nT", [P, NH, HALF])
        nTh = sb("nTh", [P, NH, HALF], F32R)
        nTl = sb("nTl", [P, NH, HALF], F32R)
        SIL, HR = 4, 6
        sil = sb("sil", [P, SIL, HALF])
        hT = sb("hT", [P, HR, HALF])
        cond_x = hT[0:G, HR - 1, :]
        big = sb("big", [P, HP * HALF])
        qg = big[:, 0:AG * HALF].rearrange("p (g t) -> p g t", g=AG)
        kj = big[:, AG * HALF:].rearrange("p (b j k) -> p b j k", b=SPH, j=4)
        qT = big[:, :].rearrange("p (c t) -> p c t", c=HP)
        sq = sb("sq", [P, 4, HALF])
        ssT = sb("ssT", [P, HALF])
        SMR = 5
        sm = sb("sm", [P, SMR, SM_COLS])
        bm = sb("bm", [P, 2, SM_COLS])
        bias = sb("bias", [P, SM_COLS])
        pT = sb("pT", [P, 2, 1024])
        vB = sb("vB", [P, 4, SPT * D])
        oB = sb("oB", [P, 2, P])
        vC = vB[:, :, :].rearrange("p t (b n) -> p t b n", b=SPT)
        kTb = sb("kTb", [P, SPH, KC])
        oT = sb("oT", [P, 2, HP, P])
        kt = sb("kt", [P, TPH, CD])
        kd = sb("kd", [P, TPH, 2, CD])
        tiny = sb("tiny", [P, 1200])
        used = [0]

        def small(*shape):
            n = int(np.prod(shape))
            a = tiny[:, used[0]:used[0] + n]
            used[0] += n
            if len(shape) == 2:
                return a.rearrange("p (a b) -> p a b", a=shape[0])
            return a

        rt_max = small(TPH)
        rt_p = [small(TPH, E) for _ in range(2)]
        rt_a, rt_b, rt_c, rt_d = (small(TPH, E) for _ in range(4))
        rt_s = small(TPH)
        rt_w = [small(TPH, E) for _ in range(2)]
        rt_hi = sb("rt_hi", [P, TPH, E], F32R)
        wpk = [small(TPH, 2 * E) for _ in range(2)]
        wTr = sb("wTr", [16, NH, HALF], F32R)
        b_max = [small(SEQ) for _ in range(2)]
        b_sum = [small(SEQ) for _ in range(2)]
        c_max = [small(CH) for _ in range(2)]
        c_sum = [small(CH) for _ in range(2)]
        rq = small(NH, TPH * CH)
        stats = small(TPH, 6)
        mean_var = [small(TPH, 2) for _ in range(2)]
        rstd = [small(TPH) for _ in range(2)]
        ssk = small(TPH)
        rk = small(TPH)
        zstats = small(2, 6)
        zmv = small(2 * TPH, 2)
        zvar = small(2 * TPH)
        zr = small(2 * TPH)
        fss = [small(TPH) for _ in range(2)]
        fr = [small(TPH) for _ in range(2)]
        kscale8 = small(1)
        nk = small(4)
        rel = sb("rel", [SEQ, D])
        relT = sb("relT", [P, SEQ])
        rel_s = small(16)
        rel_h = small(CH)
        mask_u8 = sb("mask_u8", [P, TILES * SEQ], U8)
        mneg = sb("mneg", [P, TILES, SEQ])

        d_const, d_low, d_a, d_c, d_b, d_row, d_mask, d_null = (
            sem(f"d_{n}") for n in ("const", "low", "a", "c", "b", "row", "mask", "null"))
        d_x = [sem(f"d_x{i}") for i in range(NH)]
        d_wq = [sem(f"d_wq{i}") for i in range(2)]
        d_13 = [sem(f"d_13_{i}") for i in range(4)]
        d_w2, d_wout, d_out = sem("d_w2"), sem("d_wout"), sem("d_out")
        pe_filled = sem("pe_filled")
        bank_read = [sem(f"bank_read{i}") for i in range(BANKS)]
        dve_chain, act_chain, pool_chain = sem("dve_chain"), sem("act_chain"), sem("pool_chain")
        s = {n: sem("s_" + n) for n in (
            "consts_r", "cond", "rt_exp", "wpk", "leaky", "xb", "b_exp", "b_rsum", "p_norm", "var", "rstd", "xn", "n_hi",
            "n_lo", "kss", "rk", "kd", "sq", "ssmm", "rq_sqrt", "rq", "bm", "bias", "c_add", "c_sub", "c_exp",
            "c_rsum", "c_norm", "zvar", "zr", "z", "fss", "fr", "zn", "wq_hi", "wq_lo", "w13_hi", "w13_lo",
            "rel_silu_in", "rel_silu", "relvar", "relr", "null_sq", "null_p", "null_kT", "outrow",
            "kscale", "mneg", "zero")}

        def tokens_of(v, pairs=HP):
            return v.rearrange("p (c n) -> p c n", c=pairs)[:, :, 0:2 * SEQ].rearrange("p c (a k) -> p c a k", a=2)

        def nulls_of(v, pairs=HP):
            return v.rearrange("p (c n) -> p c n", c=pairs)[:, :, 2 * SEQ:KC]

        def over_keys(v, pairs=HP):
            return v.rearrange("p (c a) -> p c a", a=2).unsqueeze(3).broadcast_to([P, pairs, 2, SEQ])

        def bank_of(step):
            return bank[NUMBER[step] % BANKS]

        def filled(eng, step):
            eng.wait_ge(pe_filled, NUMBER[step] + 1)

        def read_out(ins, step):
            ins.then_inc(bank_read[NUMBER[step] % BANKS], 1)

        def was_read(eng, step):
            n = NUMBER[step]
            eng.wait_ge(bank_read[n % BANKS], n // BANKS + 1)

        def order(kind):
            return {st[1:]: n + 1 for n, st in enumerate(st for st in PLAN if st[0] == kind)}

        u_order, g_order, ga_order, f_order = order("u"), order("g"), order("ga"), order("fn")
        g_list, ga_list = list(g_order), list(ga_order)
        n_order = {st: n + 1 for n, st in enumerate(st for st in PLAN if st[0] in ("xn", "fT"))}
        soft = [st for st in PLAN if st[0] in ("bs", "ca")]
        soft_n = {(st[0], *st[1:]): n for n, st in enumerate(soft)}

        def sm_slot(kind, h, t):
            return soft_n[(kind, h, t)] % SMR

        def sm_user_before(kind, h, t):
            n = soft_n[(kind, h, t)] - SMR
            if n < 0:
                return None
            k, hh, tt = soft[n]
            return ("bt", hh, tt) if k == "bs" else ("ct", hh, tt, 1)

        block = ctx.enter_context(nc.Block())

        @block.sync
        def _(sp):
            xv = x.rearrange("(t p) d -> p t d", p=P)
            sp.dma_start(c_sb[:, 0:WIDE_CONSTS], consts[:, 0:WIDE_CONSTS]).then_inc(d_const, 16)
            sp.dma_start(xb[:, 0:TPH], xv[:, 0:TPH]).then_inc(d_x[0], 16)
            sp.dma_start(g_sb[:], pack_c).then_inc(d_c, 16)
            sp.dma_start(a_sb[:], pack_a).then_inc(d_a, 16)
            sp.dma_start(xb[:, TPH:], xv[:, TPH:]).then_inc(d_x[1], 16)
            sp.dma_start(r_sb[:], rows.broadcast_to([P, ROW_W])).then_inc(d_row, 16)
            sp.dma_start(b_sb[:], pack_b).then_inc(d_b, 16)
            sp.dma_start(c_sb[0:SEQ, WIDE_CONSTS:], consts[0:SEQ, WIDE_CONSTS:]).then_inc(d_low, 16)
            for b in range(SPT):
                src = key_mask.rearrange("(t b) k -> b t k", b=SPT)[b:b + 1].broadcast_to([SEQ, TILES, SEQ])
                sp.dma_start(mask_u8[b * SEQ:(b + 1) * SEQ, :].rearrange("p (t k) -> p t k", k=SEQ),
                             src).then_inc(d_mask, 16)
            for n in range(2):
                sp.dma_start(sq[:, n, :], w_q[:, n * 512:(n + 1) * 512]).then_inc(d_wq[n], 16)
            for slot in range(2, 4):
                sp.dma_start(sq[:, slot, :], w13[:, slot - 2, :]).then_inc(d_13[slot], 16)
            sp.dma_start(wout_sb[:].rearrange("p c n -> p (c n)"), w_out).then_inc(d_wout, 16)
            sp.dma_start(w2_sb[:].rearrange("p e f n -> p (e f n)"), w2).then_inc(d_w2, 16)
            for e in range(2, E):
                slot = (e + 2) % 4
                if e < 4:
                    sp.wait_ge(s["wq_lo"], e - 1)
                else:
                    sp.wait_ge(s["w13_lo"], e - 3)
                sp.dma_start(sq[:, slot, :], w13[:, e, :]).then_inc(d_13[slot], 16)
            filled(sp, ("bp", NH - 1, TPH - 1))
            for slot in range(4):
                sp.dma_start(vC[64:66, slot, :, :],
                             null_v.unsqueeze(1).broadcast_to([2, SPT, P])).then_inc(d_null, 16)
            ov = out.rearrange("(t p) d -> p t d", p=P)
            for h in range(NH):
                sp.wait_ge(s["outrow"], h + 1)
                sp.dma_start(ov[:, h * TPH:(h + 1) * TPH], z[:, h * TPH:(h + 1) * TPH]).then_inc(d_out, 16)
            sp.wait_ge(d_out, 16 * NH)

        def split_load(eng, e):
            slot = (e + 2) % 4
            if slot < 2:
                eng.wait_ge(d_13[slot], 16 * (e // 4 + 1))
            else:
                eng.wait_ge(d_13[slot], 16 * (e // 4 + 1))
            return sq[:, slot, :]

        @block.tensor
        def _(pe):
            def fill(step):
                n = NUMBER[step]
                if n >= BANKS:
                    pe.wait_ge(bank_read[n % BANKS], n // BANKS)
                return bank[n % BANKS]

            def done(mm):
                mm.then_inc(pe_filled, 1)

            def three_pass(o, wh, wl, h):
                pe.matmul(o, wh, nTh[:, h, :], start=True, stop=False)
                pe.matmul(o, wl, nTh[:, h, :], start=False, stop=False)
                return pe.matmul(o, wh, nTl[:, h, :], start=False, stop=True)

            pe.wait_ge(d_const, 16)
            for st in PLAN:
                kind, a = st[0], st[1:]
                if kind not in PE_STEPS:
                    continue
                o = fill(st)
                if kind == "xT":
                    pe.wait_ge(d_x[a[0]], 16)
                    for t in range(TPH):
                        mm = pe.transpose(o[:, t * P:(t + 1) * P], xb[:, a[0] * TPH + t, :], ident)
                elif kind == "lg":
                    h, = a
                    pe.wait_ge(d_a, 16)
                    pe.wait_ge(d_c, 16)
                    was_read(pe, ("xT", h))
                    pe.wait_ge(s["cond"], h + 1)
                    for t in range(TPH):
                        oo = o[:, t * E:(t + 1) * E]
                        pe.matmul(oo, xyT[:, h, t * P:(t + 1) * P], wt, start=True, stop=False)
                        mm = pe.matmul(oo, cond_x[:, t * P:(t + 1) * P], g_sb[:, NSEQ:NSEQ + E], start=False, stop=True)
                elif kind in ("ga", "ua"):
                    h, u = a
                    if u == PAIRS:
                        w = pack_a_at("s_gate" if kind == "ga" else "s_up")
                    else:
                        w = (gate if kind == "ga" else up)[:, u, :]
                    mm = pe.matmul(o[:], w, xyT[:, h, :], start=True, stop=True)
                elif kind == "wT":
                    h, = a
                    pe.wait_ge(s["wpk"], h + 1)
                    for t in range(TPH):
                        mm = pe.transpose(o[0:2 * E, t * P:(t + 1) * P], wpk[h][:, t, :], ident)
                elif kind == "wB":
                    h, u = a
                    pe.wait_ge(s["consts_r"], 1)
                    was_read(pe, ("wT", h))
                    mm = pe.matmul(o[:], sel_r[:, u * P:(u + 1) * P], wTr[:, h, :], start=True, stop=True)
                elif kind == "yT":
                    h, = a
                    for i in range(PAIRS):
                        was_read(pe, ("wB", h, i))
                    pe.matmul(o[:], pack_a_at("s_down"), hT[:, PAIRS, :], start=True, stop=False)
                    for u in range(PAIRS):
                        mm = pe.matmul(o[:], down[:, u, :], hT[:, u, :], start=False, stop=(u == PAIRS - 1))
                elif kind in ("relT1", "relT2"):
                    pe.wait_ge(s["rel_silu"], 1 if kind == "relT1" else 2)
                    mm = pe.transpose(o[:, 0:SEQ], rel[:, :], ident[0:SEQ, 0:SEQ])
                elif kind == "relM1":
                    pe.wait_ge(d_b, 16)
                    was_read(pe, ("relT1",))
                    mm = pe.matmul(o[0:SEQ, 0:D], relT[:, :], pack_b_at("rel_w1"), start=True, stop=True)
                elif kind == "relM2":
                    was_read(pe, ("relT2",))
                    mm = pe.matmul(o[0:SEQ, 0:CH], relT[:, :], pack_b_at("rel_w2"), start=True, stop=True)
                elif kind == "bias":
                    was_read(pe, ("relM2",))
                    pe.wait_ge(d_low, 16)
                    for k in range(a[0] * 16, a[0] * 16 + 16):
                        shift = const("toeplitz", SEQ)[:, 31 - k:63 - k]
                        for b in range(SPT):
                            mm = pe.matmul(o[b * SEQ:(b + 1) * SEQ, (k % 16) * CH:(k % 16 + 1) * CH], shift,
                                           rel_h[0:SEQ, :], start=True, stop=True)
                elif kind == "null":
                    pe.wait_ge(s["null_sq"], 1)
                    mm = pe.matmul(o[:, 0:1], const("ones_h2"), nk[:, 0:1], start=True, stop=True)
                elif kind in ("bq", "bk"):
                    h, = a
                    was_read(pe, ("yT", h))
                    pe.wait_ge(d_b, 16)
                    w = wqkv[:, 0:D] if kind == "bq" else wqkv[:, D:2 * D]
                    mm = pe.matmul(o[:], w, xyT[:, h, :], start=True, stop=True)
                elif kind == "bv":
                    h, t = a
                    for b in range(SPT):
                        y_b = xyT[:, h, t * P + b * SEQ:t * P + (b + 1) * SEQ]
                        for j in range(4):
                            w = wqkv[:, 2 * D:].rearrange("p (g j d) -> p g j d", g=AG, j=4)[:, :, j, :]
                            mm = pe.matmul(o[32 * j:32 * j + 32, b * SEQ:(b + 1) * SEQ], y_b, w,
                                           start=True, stop=True)
                elif kind == "bs":
                    h, t = a
                    was_read(pe, ("bq", h))
                    was_read(pe, ("bk", h))
                    for g in range(AG):
                        for b in range(SPT):
                            q0 = t * P + b * SEQ
                            mm = pe.matmul(o[b * SEQ:(b + 1) * SEQ, g * P:(g + 1) * P], qg[:, g, q0:q0 + SEQ],
                                           kj[:, t * SPT + b, :, :], start=True, stop=True)
                elif kind == "bt":
                    h, t = a
                    pe.wait_ge(s["p_norm"], h * TPH + t + 1)
                    src = sm[:, sm_slot("bs", h, t), :]
                    for g in range(AG):
                        mm = pe.transpose(o[:, g * P:(g + 1) * P], src[:, g * P:(g + 1) * P], ident)
                elif kind == "bp":
                    h, t = a
                    was_read(pe, ("bt", h, t))
                    was_read(pe, ("bv", h, t))
                    v = vB[:, t, :].rearrange("p (b n) -> p b n", b=SPT)
                    p = pT[:, t % 2, 0:HALF]
                    for b in range(SPT):
                        for g in range(AG):
                            mm = pe.matmul(o[g * 32:(g + 1) * 32, b * SEQ:(b + 1) * SEQ],
                                           v[:, b, g * 32:(g + 1) * 32],
                                           p[:, g * P + b * SEQ:g * P + (b + 1) * SEQ], start=True, stop=True)
                elif kind == "bo":
                    h, t = a
                    was_read(pe, ("bp", h, t))
                    mm = pe.matmul(o[:, 0:D], oB[:, t % 2, :], wproj, start=True, stop=True)
                elif kind == "xn":
                    h, = a
                    pe.wait_ge(s["xn"], h + 1)
                    for t in range(TPH):
                        mm = pe.transpose(o[:, t * P:(t + 1) * P], z[:, h * TPH + t, :], ident)
                elif kind == "ck":
                    h, = a
                    was_read(pe, ("xn", h))
                    for t in range(TPH):
                        mm = pe.matmul(o[:, t * CD:(t + 1) * CD], nT[:, h, t * P:(t + 1) * P], pack_b_at("wk"),
                                       start=True, stop=True)
                elif kind == "cv":
                    h, t = a
                    for b in range(SPT):
                        n_b = nT[:, h, t * P + b * SEQ:t * P + (b + 1) * SEQ]
                        for h2 in range(2):
                            mm = pe.matmul(o[32 * h2:32 * h2 + 32, b * CD:(b + 1) * CD], n_b, pack_b_at("wv"),
                                           start=True, stop=True)
                elif kind == "kT":
                    h, = a
                    pe.wait_ge(s["kd"], h + 1)
                    for t in range(TPH):
                        mm = pe.transpose(o[:, t * P:(t + 1) * P], kd[:, t, :, :].rearrange("p a d -> p (a d)"),
                                          ident)
                elif kind == "cq":
                    h, hp = a
                    pe.wait_ge(s["n_lo"], n_order[("xn", h)])
                    pe.wait_ge(s["wq_lo"], hp // 4 + 1)
                    mm = three_pass(o[:], wqh[:, hp * P:(hp + 1) * P], wql[:, hp * P:(hp + 1) * P], h)
                elif kind == "ss":
                    h, = a
                    for hp in range(HP):
                        pe.wait_ge(s["sq"], h * HP + hp + 1)
                        j, half = hp // 2, hp % 2
                        mm = pe.matmul(o[32 * j:32 * j + 32, :], const("ones_pair")[:, 32 * half:32 * half + 32],
                                       sq[:, hp % 4, :], start=(half == 0), stop=(half == 1))
                        if hp < HP - 1:
                            mm.then_inc(s["ssmm"], 1)
                elif kind == "s2":
                    h, = a
                    was_read(pe, ("ss", h))
                    for t in range(TPH):
                        mm = pe.transpose(o[:, t * P:(t + 1) * P], ssT[:, t * P:(t + 1) * P], ident)
                elif kind == "cs":
                    h, t, c = a
                    was_read(pe, ("kT", h))
                    pe.wait_ge(s["null_kT"], 2)
                    for i in range(4):
                        hp = 4 * c + i
                        if t == 0:
                            was_read(pe, ("cq", h, hp))
                        for b in range(SPT):
                            q0 = t * P + b * SEQ
                            mm = pe.matmul(o[b * SEQ:(b + 1) * SEQ, i * KC:(i + 1) * KC], qT[:, hp, q0:q0 + SEQ],
                                           kTb[:, t * SPT + b, :], start=True, stop=True)
                elif kind == "ct":
                    h, t, c = a
                    pe.wait_ge(s["c_norm"], h * TPH + t + 1)
                    src = sm[:, sm_slot("ca", h, t), :]
                    for i in range(4):
                        mm = pe.transpose(o[0:KC, i * P:(i + 1) * P], src[:, (4 * c + i) * KC:(4 * c + i + 1) * KC],
                                          ident)
                elif kind == "cp":
                    h, t, c = a
                    was_read(pe, ("ct", h, t, 0))
                    was_read(pe, ("ct", h, t, 1))
                    was_read(pe, ("cv", h, t))
                    pe.wait_ge(d_null, 16 * 4)
                    p = pT[0:KC, t % 2, :].rearrange("p (c n) -> p c n", c=HP)
                    for i in range(2):
                        b = 2 * c + i
                        mm = pe.matmul(o[:, i * 256:(i + 1) * 256], vC[0:KC, t, b, :],
                                       p[:, :, b * SEQ:(b + 1) * SEQ], start=True, stop=True)
                elif kind == "co":
                    h, t = a
                    was_read(pe, ("cp", h, t, 0))
                    was_read(pe, ("cp", h, t, 1))
                    pe.wait_ge(d_wout, 16)
                    for hp in range(HP):
                        mm = pe.matmul(o[:, 0:D], oT[:, t % 2, hp, :], wout_sb[:, hp, :], start=(hp == 0),
                                       stop=(hp == HP - 1))
                elif kind == "fT":
                    l, h = a
                    pe.wait_ge(s["zn"], f_order[(l, h)])
                    for t in range(TPH):
                        mm = pe.transpose(o[:, t * P:(t + 1) * P], xyT[:, h, t * P:(t + 1) * P], ident)
                elif kind == "fr":
                    l, h = a
                    was_read(pe, ("fT", l, h))
                    for t in range(TPH):
                        mm = pe.matmul(o[:, t * E:(t + 1) * E], nT[:, h, t * P:(t + 1) * P], pack_b_at("router"),
                                       start=True, stop=True)
                elif kind in ("g", "u"):
                    l, h, e, f = a
                    pe.wait_ge(s["n_lo"], n_order[("fT", l, h)])
                    pe.wait_ge(s["w13_lo"], e + 1)
                    c0 = f * P + (F if kind == "u" else 0)
                    mm = three_pass(o[:], w13h[:, e, c0:c0 + P], w13l[:, e, c0:c0 + P], h)
                elif kind == "y":
                    l, h, e = a
                    pe.wait_ge(d_w2, 16)
                    for t in range(TPH):
                        for f in range(FC):
                            n = u_order[(l, h, e, f)]
                            if t == 0:
                                was_read(pe, ("u", l, h, e, f))
                            mm = pe.matmul(o[:, t * D:(t + 1) * D], hT[:, (n - 1) % HR, t * P:(t + 1) * P],
                                           w2_sb[:, e, f, :], start=(f == 0), stop=(f == FC - 1))
                done(mm)

        @block.scalar
        def _(act):
            def copy(o, i, **k):
                return act.activation(o, i, ACT.Copy, **k)

            act.wait_ge(d_const, 16)
            for st in PLAN:
                kind, a = st[0], st[1:]
                if kind == "xT":
                    filled(act, st)
                    read_out(copy(xyT[:, a[0], :], bank_of(st)[:]), st)
                elif kind == "lg":
                    h, = a
                    was_read(act, st)
                    act.activation(rt_p[h], rt_p[h], ACT.Exp, scale=0.5).then_inc(s["rt_exp"], 1)
                elif kind == "ga":
                    filled(act, st)
                    n = ga_order[a]
                    if n > SIL:
                        was_read(act, ("ua", *ga_list[n - SIL - 1]))
                    read_out(copy(sil[:, (n - 1) % SIL, :], bank_of(st)[:]), st)
                elif kind == "wT":
                    filled(act, st)
                    read_out(copy(wTr[:, a[0], :], bank_of(st)[0:2 * E, :]), st)
                elif kind == "yT":
                    filled(act, st)
                    read_out(copy(xyT[:, a[0], :], bank_of(st)[:]), st)
                elif kind in ("rel1", "relM1"):
                    act.wait_ge(s["rel_silu_in"], 1 if kind == "rel1" else 2)
                    act.activation(rel[:, :], rel[:, :], ACT.Silu).then_inc(s["rel_silu"], 1)
                elif kind in ("relT1", "relT2"):
                    filled(act, st)
                    read_out(copy(relT[:, :], bank_of(st)[:, 0:SEQ]), st)
                elif kind == "bq":
                    h, = a
                    filled(act, st)
                    if h:
                        filled(act, ("bs", h - 1, TPH - 1))
                    for g in range(AG):
                        ins = copy(qg[:, g, :], bank_of(st)[:], scale=const("mask_g")[:, g:g + 1])
                    read_out(ins, st)
                elif kind == "bk":
                    h, = a
                    filled(act, st)
                    if h:
                        filled(act, ("bs", h - 1, TPH - 1))
                    for j in range(4):
                        ins = copy(kj[:, :, j, :], bank_of(st)[:].rearrange("p (b k) -> p b k", b=SPH),
                                   scale=const("mask_j")[:, j:j + 1])
                    read_out(ins, st)
                elif kind == "bs":
                    h, t = a
                    was_read(act, st)
                    v = sm[:, sm_slot("bs", h, t), 0:HALF]
                    act.activation(v, v, ACT.Exp).then_inc(s["b_exp"], 1)
                elif kind == "bt":
                    h, t = a
                    filled(act, st)
                    n = h * TPH + t
                    if n >= 2:
                        filled(act, ("bp", (n - 2) // TPH, (n - 2) % TPH))
                    read_out(copy(pT[:, t % 2, 0:HALF], bank_of(st)[:]), st)
                elif kind == "bp":
                    h, t = a
                    filled(act, st)
                    n = h * TPH + t
                    if n >= 2:
                        filled(act, ("bo", (n - 2) // TPH, (n - 2) % TPH))
                    read_out(copy(oB[:, t % 2, :], bank_of(st)[:, 0:P]), st)
                elif kind == "xn":
                    filled(act, st)
                    read_out(copy(nT[:, a[0], :], bank_of(st)[:], scale=column("g_norm")), st)
                elif kind == "kT":
                    h, = a
                    filled(act, st)
                    act.wait_ge(s["kscale"], 1)
                    act.wait_ge(s["zero"], 1)
                    if h:
                        filled(act, ("cs", h - 1, TPH - 1, 1))
                    for h2 in range(2):
                        r = slice(64 * h2, 64 * h2 + 64)
                        src = bank_of(st)[r, :].rearrange("p (b k) -> p b k", b=SPH)
                        dst = kTb[r, :, h2 * SEQ:(h2 + 1) * SEQ]
                        ins = copy(dst, src, scale=kscale8[r, :])
                    read_out(ins, st)
                elif kind == "cq":
                    h, hp = a
                    filled(act, st)
                    if h:
                        filled(act, ("cs", h - 1, TPH - 1, 1))
                    else:
                        filled(act, ("bs", NH - 1, TPH - 1))
                    read_out(copy(qT[:, hp, :], bank_of(st)[:]), st)
                elif kind == "s2":
                    h, = a
                    was_read(act, st)
                    act.activation(rq[:, h, :], rq[:, h, :], ACT.Sqrt).then_inc(s["rq_sqrt"], 1)
                elif kind == "cm":
                    h, t = a
                    act.wait_ge(s["c_sub"], h * TPH + t + 1)
                    v = sm[:, sm_slot("ca", h, t), :]
                    act.activation(v, v, ACT.Exp).then_inc(s["c_exp"], 1)
                elif kind == "ct":
                    h, t, c = a
                    filled(act, st)
                    n = h * TPH + t
                    if n >= 2:
                        filled(act, ("cp", (n - 2) // TPH, (n - 2) % TPH, 1))
                    else:
                        filled(act, ("bp", NH - 1, TPH - 2 + n))
                    read_out(copy(pT[0:KC, t % 2, c * HALF:(c + 1) * HALF], bank_of(st)[0:KC, :]), st)
                elif kind == "fT":
                    filled(act, st)
                    read_out(copy(nT[:, a[1], :], bank_of(st)[:], scale=column("norm_w")), st)
                elif kind == "fr":
                    l, h = a
                    was_read(act, st)
                    act.activation(rt_p[h], rt_p[h], ACT.Exp).then_inc(s["rt_exp"], 1)
                elif kind == "g":
                    n = g_order[a]
                    filled(act, st)
                    if n > SIL:
                        was_read(act, ("u", *g_list[n - SIL - 1]))
                    read_out(act.activation(sil[:, (n - 1) % SIL, :], bank_of(st)[:], ACT.Silu), st)

        @block.gpsimd
        def _(pool):
            n_chain = [0]

            def link(ins):
                n_chain[0] += 1
                ins.then_inc(pool_chain, 1)
                pool.wait_ge(pool_chain, n_chain[0])

            power = const("power")
            pool.memset(kTb[:, :, :], 0.0).then_inc(s["zero"], 1)
            pool.wait_ge(d_const, 16)
            for st in PLAN:
                kind, a = st[0], st[1:]
                if kind == "lg":
                    h, = a
                    pool.wait_ge(d_c, 16)
                    if h:
                        filled(pool, ("lg", h - 1))
                    c = g_sb[:, h * SPH:(h + 1) * SPH].unsqueeze(2).broadcast_to([G, SPH, SEQ])
                    pool.tensor_copy(cond_x.rearrange("g (b t) -> g b t", b=SPH), c).then_inc(s["cond"], 1)
                elif kind == "w":
                    h, = a
                    pool.wait_ge(d_row, 16)
                    filled(pool, ("xT", h))
                    v = xb[:, h * TPH:(h + 1) * TPH, :]
                    pool.tensor_tensor(v, v, row("b_proj").unsqueeze(1).broadcast_to([P, TPH, D]),
                                       ALU.add).then_inc(s["xb"], 1)
                elif kind == "rel1" or kind == "relM1":
                    n = 1 if kind == "rel1" else 2
                    pool.wait_ge(s["relvar"], n)
                    pool.tensor_tensor(rel_s[0:SEQ, 9:10], rel_s[0:SEQ, 8:9], power[0:SEQ, 0:1],
                                       ALU.pow).then_inc(s["relr"], 1)
                elif kind == "null":
                    was_read(pool, st)
                    pool.tensor_tensor(nk[:, 2:3], nk[:, 1:2], power[:, 0:1], ALU.pow).then_inc(s["null_p"], 1)
                elif kind == "bn":
                    h, t = a
                    n = h * TPH + t + 1
                    pool.wait_ge(s["b_rsum"], n)
                    v = sm[:, sm_slot("bs", h, t), 0:HALF].rearrange("p (h k) -> p h k", h=AH)
                    r = b_sum[n % 2].unsqueeze(1).broadcast_to([P, AH, SEQ])
                    pool.tensor_tensor(v, v, r, ALU.mult).then_inc(s["p_norm"], 1)
                elif kind == "ln":
                    h, = a
                    pool.wait_ge(s["var"], h + 1)
                    pool.tensor_tensor(rstd[h], rstd[h], power[:, 0:TPH], ALU.pow).then_inc(s["rstd"], 1)
                elif kind == "ck":
                    h, = a
                    pool.wait_ge(s["kss"], h + 1)
                    pool.tensor_tensor(rk, ssk, power[:, 0:TPH], ALU.pow).then_inc(s["rk"], 1)
                elif kind in ("split_q", "split"):
                    if kind == "split_q":
                        n, = a
                        pool.wait_ge(s["wq_hi"], n + 1)
                        pool.tensor_tensor(wql[:, n * 512:(n + 1) * 512], sq[:, n, :],
                                           wqh[:, n * 512:(n + 1) * 512].bitcast(F32),
                                           ALU.subtract).then_inc(s["wq_lo"], 1)
                    else:
                        e, = a
                        src = split_load(pool, e)
                        pool.wait_ge(s["w13_hi"], e + 1)
                        pool.tensor_tensor(w13l[:, e, :], src, w13h[:, e, :].bitcast(F32),
                                           ALU.subtract).then_inc(s["w13_lo"], 1)
                elif kind == "bm":
                    h, t = a
                    n = h * TPH + t
                    was_read(pool, ("bias", 1))
                    pool.wait_ge(s["bias"], 1)
                    pool.wait_ge(s["mneg"], 1)
                    if n >= 2:
                        pool.wait_ge(s["c_add"], n - 1)
                    if n < 2:
                        pool.tensor_copy(nulls_of(bm[:, n % 2, :]), nulls_of(bias[:, :])).then_inc(s["bm"], 1)
                    keys = mneg[:, n, :].unsqueeze(1).unsqueeze(2).broadcast_to([P, HP, 2, SEQ])
                    pool.tensor_tensor(tokens_of(bm[:, n % 2, :]), tokens_of(bias[:, :]), keys,
                                       ALU.add).then_inc(s["bm"], 1)
                elif kind == "ca":
                    h, t = a
                    n = h * TPH + t + 1
                    was_read(pool, ("cs", h, t, 0))
                    was_read(pool, ("cs", h, t, 1))
                    pool.wait_ge(s["bm"], n + min(n, 2))
                    v = sm[:, sm_slot("ca", h, t), :]
                    pool.tensor_tensor(v, v, bm[:, (n - 1) % 2, :], ALU.add).then_inc(s["c_add"], 1)
                elif kind == "cn":
                    h, t = a
                    n = h * TPH + t + 1
                    pool.wait_ge(s["c_rsum"], n)
                    v = sm[:, sm_slot("ca", h, t), :]
                    r = c_sum[n % 2]
                    pool.tensor_tensor(nulls_of(v), nulls_of(v), r.rearrange("p (c a) -> p c a", a=2), ALU.mult)
                    pool.tensor_tensor(tokens_of(v), tokens_of(v), over_keys(r), ALU.mult).then_inc(s["c_norm"], 1)
                elif kind == "co":
                    h, t = a
                    i = h * TPH + t
                    pool.wait_ge(s["zvar"], i + 1)
                    pool.tensor_tensor(zr[:, i:i + 1], zvar[:, i:i + 1], power[:, 0:1],
                                       ALU.pow).then_inc(s["zr"], 1)
                elif kind == "fn":
                    l, h = a
                    pool.wait_ge(s["fss"], f_order[a])
                    pool.tensor_tensor(fr[h], fss[h], power[:, 0:TPH], ALU.pow).then_inc(s["fr"], 1)

        @block.vector
        def _(dve):
            n_chain = [0]

            def link(ins):
                n_chain[0] += 1
                ins.then_inc(dve_chain, 1)
                dve.wait_ge(dve_chain, n_chain[0])

            def route_start(st, h):
                filled(dve, st)
                lv = bank_of(st)[:, 0:TPH * E].rearrange("p (t e) -> p t e", t=TPH)
                link(dve.tensor_reduce(rt_max, lv, AX_X, ALU.max))
                ins = dve.tensor_tensor(rt_p[h], lv, rt_max.unsqueeze(2).broadcast_to([P, TPH, E]), ALU.subtract)
                read_out(ins, st)

            def over(v):
                return v.unsqueeze(2).broadcast_to([P, TPH, E])

            def route_finish(h, count, eps):
                p, w = rt_p[h], rt_w[h]
                rank = const("rank").unsqueeze(1).broadcast_to([P, TPH, E])
                dve.wait_ge(s["rt_exp"], count)
                link(dve.tensor_reduce(rt_s, p, AX_X, ALU.add))
                link(dve.reciprocal(rt_s, rt_s))
                link(dve.tensor_tensor(p, p, over(rt_s), ALU.mult))

                def best(src, taken):
                    link(dve.tensor_reduce(rt_s, src, AX_X, ALU.max))
                    link(dve.tensor_tensor(rt_a, src, over(rt_s), ALU.is_equal))
                    link(dve.tensor_tensor(rt_a, rt_a, rank, ALU.mult))
                    link(dve.tensor_reduce(rt_s, rt_a, AX_X, ALU.max))
                    link(dve.tensor_tensor(taken, rt_a, over(rt_s), ALU.is_equal))

                best(p, rt_b)
                link(dve.scalar_tensor_tensor(rt_d, rt_b, -2.0, p, ALU.mult, ALU.add))
                best(rt_d, rt_c)
                link(dve.tensor_tensor(rt_b, rt_b, rt_c, ALU.add))
                link(dve.tensor_tensor(rt_b, rt_b, p, ALU.mult))
                link(dve.tensor_reduce(rt_s, rt_b, AX_X, ALU.add))
                link(dve.tensor_scalar(rt_s, rt_s, eps, None, ALU.add))
                link(dve.reciprocal(rt_s, rt_s))
                link(dve.tensor_tensor(w, rt_b, over(rt_s), ALU.mult))

            def rel_norm(src, gain, add, n):
                r = rel[:, :]
                if add is not None:
                    link(dve.tensor_tensor(r, src, row(add, SEQ), ALU.add))
                link(dve.bn_stats(rel_s[0:SEQ, 0:6], r))
                link(dve.bn_aggr(rel_s[0:SEQ, 6:8], rel_s[0:SEQ, 0:6]))
                dve.tensor_scalar(rel_s[0:SEQ, 8:9], rel_s[0:SEQ, 7:8], 1e-5, None, ALU.add).then_inc(s["relvar"], 1)
                dve.wait_ge(s["relr"], n)
                link(dve.tensor_scalar(r, r, rel_s[0:SEQ, 6:7], rel_s[0:SEQ, 9:10], ALU.subtract, ALU.mult))
                dve.tensor_tensor(r, r, row(gain, SEQ), ALU.mult).then_inc(s["rel_silu_in"], 1)

            def split_n(st, h):
                was_read(dve, st)
                dve.tensor_copy(nTh[:, h, :], nT[:, h, :]).then_inc(s["n_hi"], 1)
                dve.wait_ge(s["n_hi"], n_order[st])
                dve.tensor_tensor(nTl[:, h, :], nT[:, h, :], nTh[:, h, :].bitcast(F32),
                                  ALU.subtract).then_inc(s["n_lo"], 1)

            def z_norm(h, t):
                i = h * TPH + t
                dve.wait_ge(s["zr"], i + 1)
                link(dve.tensor_scalar(z[:, i, :], z[:, i, :], zmv[:, i, 0:1], zr[:, i:i + 1], ALU.subtract,
                                       ALU.mult))
                dve.tensor_tensor(z[:, i, :], z[:, i, :], row("g_out"), ALU.mult).then_inc(s["z"], 1)

            def square(h, hp):
                n = h * HP + hp
                was_read(dve, ("cq", h, hp))
                if hp >= 4:
                    dve.wait_ge(s["ssmm"], h * (HP - 1) + hp - 3)
                elif h:
                    filled(dve, ("ss", h - 1))
                else:
                    dve.wait_ge(s["w13_lo"], E)
                v = qT[:, hp, :]
                dve.tensor_tensor(sq[:, hp % 4, :], v, v, ALU.mult).then_inc(s["sq"], 1)

            dve.wait_ge(d_const, 16)
            for st in PLAN:
                kind, a = st[0], st[1:]
                if kind == "lg":
                    route_start(st, a[0])
                    if a[0] == 1:
                        dve.wait_ge(d_low, 16)
                        dve.tensor_copy(sel_r[:, :], const("select", 16)).then_inc(s["consts_r"], 1)
                elif kind == "w":
                    h, = a
                    route_finish(h, h + 1, 1e-20)
                    link(dve.tensor_copy(rt_hi[:, :, :], rt_w[h]))
                    dve.tensor_copy(wpk[h][:, :, 0:E], rt_hi[:, :, :].bitcast(F32))
                    dve.tensor_tensor(wpk[h][:, :, E:], rt_w[h], rt_hi[:, :, :].bitcast(F32),
                                      ALU.subtract).then_inc(s["wpk"], 1)
                elif kind == "ua":
                    h, u = a
                    n = ga_order[a]
                    was_read(dve, ("ga", h, u))
                    v = sil[:, (n - 1) % SIL, :]
                    dve.scalar_tensor_tensor(v, v, 0.01, v, ALU.mult, ALU.max).then_inc(s["leaky"], 1)
                    filled(dve, st)
                    if h:
                        filled(dve, ("yT", h - 1))
                    dve.wait_ge(s["leaky"], n)
                    read_out(dve.tensor_tensor(hT[:, u, :], v, bank_of(st)[:], ALU.mult), st)
                elif kind == "wB":
                    h, u = a
                    filled(dve, st)
                    was_read(dve, ("ua", h, u))
                    read_out(dve.tensor_tensor(hT[:, u, :], hT[:, u, :], bank_of(st)[:], ALU.mult), st)
                elif kind == "rel1":
                    dve.wait_ge(d_row, 16)
                    dve.wait_ge(d_low, 16)
                    link(dve.tensor_scalar(rel[:, :], row("w0", SEQ), const("position", SEQ), None, ALU.mult))
                    rel_norm(rel[:, :], "g0", "b0", 1)
                    dve.wait_ge(d_mask, 16 * SPT)
                    dve.tensor_scalar(mneg[:, :, :], mask_u8[:, :].rearrange("p (t k) -> p t k", k=SEQ),
                                      -NEG, NEG, ALU.mult, ALU.add).then_inc(s["mneg"], 1)
                elif kind == "relM1":
                    filled(dve, st)
                    r = rel[:, :]
                    read_out(dve.tensor_tensor(r, bank_of(st)[0:SEQ, 0:D], row("b1", SEQ), ALU.add), st)
                    was_read(dve, st)
                    rel_norm(r, "g1", None, 2)
                elif kind == "relM2":
                    filled(dve, st)
                    read_out(dve.tensor_tensor(rel_h[0:SEQ, :], bank_of(st)[0:SEQ, 0:CH], row("b2", SEQ), ALU.add),
                             st)
                elif kind == "bias":
                    filled(dve, st)
                    k0 = a[0] * 16
                    out_v = tokens_of(bias[:, :])[:, :, :, k0:k0 + 16].rearrange("p c a k -> p k c a")
                    pv = bank_of(st)[:, 0:16 * CH].rearrange("p (k c a) -> p k c a", k=16, a=2)
                    cv = const("causal")[:, k0:k0 + 16].unsqueeze(2).unsqueeze(3).broadcast_to([P, 16, HP, 2])
                    read_out(dve.tensor_tensor(out_v, pv, cv, ALU.add), st)
                    if a[0] == 1:
                        dve.tensor_copy(nulls_of(bias[:, :]), row("null_bias").rearrange("p (c a) -> p c a", a=2)
                                        ).then_inc(s["bias"], 1)
                elif kind == "null":
                    dve.wait_ge(d_b, 16)
                    dve.tensor_scalar(kscale8[:, :], column("k_scale"), column("q_scale"), 8.0, ALU.mult,
                                      ALU.mult).then_inc(s["kscale"], 1)
                    dve.tensor_tensor(nk[:, 0:1], column("null_k"), column("null_k"),
                                      ALU.mult).then_inc(s["null_sq"], 1)
                    filled(dve, st)
                    ins = dve.tensor_scalar(nk[:, 1:2], bank_of(st)[:, 0:1], 1e-24, None, ALU.max)
                    read_out(ins, st)
                    dve.wait_ge(s["null_p"], 1)
                    dve.wait_ge(s["kscale"], 1)
                    link(dve.tensor_scalar(nk[:, 3:4], column("null_k"), nk[:, 2:3], kscale8[:, :], ALU.mult,
                                           ALU.mult))
                    dve.wait_ge(s["zero"], 1)
                    for h2 in range(2):
                        r = slice(64 * h2, 64 * h2 + 64)
                        dve.tensor_copy(kTb[r, :, 2 * SEQ + h2:2 * SEQ + h2 + 1],
                                        nk[r, 3:4].unsqueeze(1).broadcast_to([64, SPH, 1])).then_inc(s["null_kT"], 1)
                elif kind == "bv":
                    h, t = a
                    filled(dve, st)
                    if h:
                        filled(dve, ("bp", h - 1, t))
                    v = vB[:, t, :].rearrange("p (n j d) -> p n j d", j=4, d=AD)
                    pv = bank_of(st)[:, 0:D].rearrange("p (n d) -> p n d", d=AD)
                    n = SPT * AG
                    read_out(dve.tensor_tensor(
                        v, pv.unsqueeze(2).broadcast_to([P, n, 4, AD]),
                        const("mask_v").unsqueeze(1).unsqueeze(3).broadcast_to([P, n, 4, AD]), ALU.mult), st)
                elif kind == "bs":
                    h, t = a
                    filled(dve, st)
                    before = sm_user_before("bs", h, t)
                    if before:
                        filled(dve, before)
                    n = h * TPH + t
                    if n >= 2:
                        was_read(dve, ("bs", (n - 2) // TPH, (n - 2) % TPH))
                    pv = bank_of(st)[:].rearrange("p (h k) -> p h k", h=AH)
                    link(dve.tensor_reduce(b_max[n % 2], bank_of(st)[:].rearrange("p (h k) -> p k h", h=AH), AX_X, ALU.max))
                    v = sm[:, sm_slot("bs", h, t), 0:HALF].rearrange("p (h k) -> p h k", h=AH)
                    read_out(dve.tensor_tensor(v, pv, b_max[n % 2].unsqueeze(1).broadcast_to([P, AH, SEQ]), ALU.subtract),
                             st)
                elif kind == "bn":
                    h, t = a
                    n = h * TPH + t + 1
                    dve.wait_ge(s["b_exp"], n)
                    if n > 2:
                        dve.wait_ge(s["p_norm"], n - 2)
                    v = sm[:, sm_slot("bs", h, t), 0:HALF].rearrange("p (h k) -> p k h", h=AH)
                    link(dve.tensor_reduce(b_sum[n % 2], v, AX_X, ALU.add))
                    dve.reciprocal(b_sum[n % 2], b_sum[n % 2]).then_inc(s["b_rsum"], 1)
                elif kind == "bo":
                    h, t = a
                    filled(dve, st)
                    dve.wait_ge(s["xb"], h + 1)
                    v = xb[:, h * TPH + t, :]
                    read_out(dve.tensor_tensor(v, v, bank_of(st)[:, 0:D], ALU.add), st)
                elif kind == "ln":
                    h, = a
                    for t in range(TPH):
                        was_read(dve, ("bo", h, t))
                        link(dve.bn_stats(stats[:, t, :], xb[:, h * TPH + t, :]))
                        ins = dve.bn_aggr(mean_var[h][:, t, :], stats[:, t, :])
                    link(ins)
                    dve.tensor_scalar(rstd[h], mean_var[h][:, :, 1], 1e-5, None, ALU.add).then_inc(s["var"], 1)
                elif kind == "ln2":
                    h, = a
                    dve.wait_ge(s["rstd"], h + 1)
                    for t in range(TPH):
                        ins = dve.tensor_scalar(z[:, h * TPH + t, :], xb[:, h * TPH + t, :], mean_var[h][:, t, 0:1],
                                                rstd[h][:, t:t + 1], ALU.subtract, ALU.mult)
                    ins.then_inc(s["xn"], 1)
                elif kind == "xn":
                    split_n(st, a[0])
                elif kind == "ck":
                    h, = a
                    filled(dve, st)
                    read_out(dve.tensor_copy(kt[:, :, :], bank_of(st)[:, 0:TPH * CD].rearrange("p (t d) -> p t d",
                                                                                             t=TPH)), st)
                    was_read(dve, st)
                    if h:
                        filled(dve, ("kT", h - 1))
                    link(dve.tensor_tensor(kd[:, :, 0, :], kt[:, :, :], kt[:, :, :], ALU.mult))
                    link(dve.tensor_reduce(ssk, kd[:, :, 0, :], AX_X, ALU.add))
                    dve.tensor_scalar(ssk, ssk, 1e-24, None, ALU.max).then_inc(s["kss"], 1)
                elif kind == "ck2":
                    h, = a
                    dve.wait_ge(s["rk"], h + 1)
                    for i in range(2):
                        ins = dve.tensor_tensor(kd[:, :, i, :], kt[:, :, :], rk.unsqueeze(2).broadcast_to([P, TPH, CD]),
                                                ALU.mult)
                    ins.then_inc(s["kd"], 1)
                elif kind == "cv":
                    h, t = a
                    filled(dve, st)
                    if h:
                        filled(dve, ("cp", h - 1, t, 1))
                    pv = bank_of(st)[0:64, 0:SPT * CD].rearrange("p (b d) -> p b d", b=SPT)
                    read_out(dve.tensor_tensor(
                        vC[0:64, t, :, :].rearrange("p b (a d) -> p b a d", a=2),
                        pv.unsqueeze(2).broadcast_to([64, SPT, 2, CD]),
                        const("mask_vc", 64).unsqueeze(1).unsqueeze(3).broadcast_to([64, SPT, 2, CD]), ALU.mult), st)
                elif kind == "cq":
                    h, hp = a
                    if hp < 4:
                        square(h, hp)
                elif kind == "ss":
                    h, = a
                    for hp in range(4, HP):
                        square(h, hp)
                    filled(dve, st)
                    if h:
                        filled(dve, ("s2", h - 1))
                    read_out(dve.tensor_copy(ssT[:, :], bank_of(st)[:]), st)
                elif kind == "s2":
                    h, = a
                    filled(dve, st)
                    src = bank_of(st)[:].rearrange("p (t j c) -> p t j c", t=TPH, c=32)[:, :, :, 0:4]
                    dst = rq[:, h, :].rearrange("p (t j c) -> p t j c", t=TPH, c=4)
                    read_out(dve.tensor_scalar(dst, src, 1e-24, None, ALU.max), st)
                    dve.wait_ge(s["rq_sqrt"], h + 1)
                    dve.reciprocal(rq[:, h, :], rq[:, h, :]).then_inc(s["rq"], 1)
                elif kind == "cs":
                    h, t, c = a
                    filled(dve, st)
                    before = sm_user_before("ca", h, t)
                    if before:
                        filled(dve, before)
                    dve.wait_ge(s["rq"], h + 1)
                    r = rq[:, h, t * CH + c * 8:t * CH + c * 8 + 8]
                    v, pv = sm[:, sm_slot("ca", h, t), c * HC:(c + 1) * HC], bank_of(st)[:, 0:HC]
                    dve.tensor_tensor(nulls_of(v, 4), nulls_of(pv, 4), r.rearrange("p (c a) -> p c a", a=2), ALU.mult)
                    read_out(dve.tensor_tensor(tokens_of(v, 4), tokens_of(pv, 4), over_keys(r, 4), ALU.mult), st)
                elif kind == "cm":
                    h, t = a
                    n = h * TPH + t + 1
                    dve.wait_ge(s["c_add"], n)
                    v = sm[:, sm_slot("ca", h, t), :]
                    if n > 2:
                        dve.wait_ge(s["c_sub"], n - 2)
                    m = c_max[n % 2].rearrange("p (c a) -> p c a", a=2)
                    link(dve.tensor_reduce(m, tokens_of(v), AX_X, ALU.max))
                    link(dve.tensor_tensor(m, m, nulls_of(v), ALU.max))
                    dve.tensor_tensor(nulls_of(v), nulls_of(v), m, ALU.subtract)
                    dve.tensor_tensor(tokens_of(v), tokens_of(v), over_keys(c_max[n % 2]), ALU.subtract).then_inc(s["c_sub"], 1)
                elif kind == "cn":
                    h, t = a
                    n = h * TPH + t + 1
                    dve.wait_ge(s["c_exp"], n)
                    if n > 2:
                        dve.wait_ge(s["c_norm"], n - 2)
                    v = sm[:, sm_slot("ca", h, t), :]
                    total = c_sum[n % 2].rearrange("p (c a) -> p c a", a=2)
                    link(dve.tensor_reduce(total, tokens_of(v), AX_X, ALU.add))
                    link(dve.tensor_tensor(total, total, nulls_of(v), ALU.add))
                    dve.reciprocal(c_sum[n % 2], c_sum[n % 2]).then_inc(s["c_rsum"], 1)
                elif kind == "cp":
                    h, t, c = a
                    n = h * TPH + t
                    filled(dve, st)
                    if n >= 2:
                        filled(dve, ("co", (n - 2) // TPH, (n - 2) % TPH))
                    dst = oT[:, t % 2, :, c * 64:(c + 1) * 64].rearrange("p c (b q) -> p b c q", b=2)
                    src = bank_of(st)[:].rearrange("p (b c q) -> p b c q", b=2, c=HP)
                    read_out(dve.tensor_copy(dst, src), st)
                elif kind == "co":
                    h, t = a
                    i = h * TPH + t
                    filled(dve, st)
                    read_out(dve.tensor_copy(z[:, i, :], bank_of(st)[:, 0:D]), st)
                    was_read(dve, st)
                    link(dve.bn_stats(zstats[:, t % 2, :], z[:, i, :]))
                    link(dve.bn_aggr(zmv[:, i, :], zstats[:, t % 2, :]))
                    dve.tensor_scalar(zvar[:, i:i + 1], zmv[:, i, 1:2], 1e-5, None, ALU.add).then_inc(s["zvar"], 1)
                    if t:
                        z_norm(h, t - 1)
                    if t == TPH - 1:
                        z_norm(h, t)
                elif kind == "fn":
                    l, h = a
                    n = f_order[a]
                    zv = z[:, h * TPH:(h + 1) * TPH, :]
                    if l == 0:
                        dve.wait_ge(s["z"], (h + 1) * TPH)
                    else:
                        was_read(dve, ("y", l - 1, h, E - 1))
                        filled(dve, ("fT", l - 1, h))
                    t3 = xyT[:, h, :].rearrange("p (t d) -> p t d", t=TPH)
                    link(dve.tensor_tensor(t3, zv, zv, ALU.mult))
                    link(dve.tensor_reduce(fss[h], t3, AX_X, ALU.add))
                    dve.tensor_scalar(fss[h], fss[h], 1.0 / D, 1e-6, ALU.mult, ALU.add).then_inc(s["fss"], 1)
                elif kind == "fm":
                    l, h = a
                    dve.wait_ge(s["fr"], f_order[a])
                    zv = z[:, h * TPH:(h + 1) * TPH, :]
                    t3 = xyT[:, h, :].rearrange("p (t d) -> p t d", t=TPH)
                    dve.tensor_tensor(t3, zv, fr[h].unsqueeze(2).broadcast_to([P, TPH, D]),
                                      ALU.mult).then_inc(s["zn"], 1)
                elif kind == "fT":
                    split_n(st, a[1])
                elif kind == "fr":
                    route_start(st, a[1])
                elif kind == "fw":
                    route_finish(a[1], NH + f_order[a], 1e-9)
                elif kind == "u":
                    l, h, e, f = a
                    n = u_order[a]
                    was_read(dve, ("g", *a))
                    filled(dve, st)
                    if n > HR:
                        filled(dve, ("y", *g_list[n - HR - 1][:3]))
                    ins = dve.tensor_tensor(hT[:, (n - 1) % HR, :], sil[:, (n - 1) % SIL, :], bank_of(st)[:],
                                            ALU.mult)
                    read_out(ins, st)
                elif kind == "y":
                    l, h, e = a
                    filled(dve, st)
                    for t in range(TPH):
                        v = z[:, h * TPH + t, :]
                        if t == 0 and e:
                            was_read(dve, ("y", l, h, e - 1))
                        ins = dve.scalar_tensor_tensor(v, bank_of(st)[:, t * D:(t + 1) * D], rt_w[h][:, t, e:e + 1],
                                                       v, ALU.mult, ALU.add)
                    read_out(ins, st)
                elif kind == "out":
                    h, = a
                    was_read(dve, ("y", LOOPS - 1, h, E - 1))
                    sl = slice(h * TPH, (h + 1) * TPH)
                    dve.tensor_tensor(z[:, sl, :], z[:, sl, :], xb[:, sl, :], ALU.add).then_inc(s["outrow"], 1)
                elif kind == "split_q":
                    n, = a
                    dve.wait_ge(d_wq[n], 16)
                    dve.tensor_copy(wqh[:, n * 512:(n + 1) * 512], sq[:, n, :]).then_inc(s["wq_hi"], 1)
                elif kind == "split":
                    e, = a
                    src = split_load(dve, e)
                    dve.tensor_copy(w13h[:, e, :], src).then_inc(s["w13_hi"], 1)


def kernel(**inputs):
    import concourse.bacc as _bacc
    from concourse.bass_utils import run_bass_kernel_spmd as _run

    def arr(name):
        return np.asarray(inputs[name])

    def pack(table, width, parts, values):
        a = np.zeros((parts, width), np.float32)
        for name, (lo, hi) in table.items():
            a[:, lo:hi] = values[name].reshape(parts, hi - lo)
        return a

    cond = arr("cond_64")
    pairs = lambda w: w.reshape(PAIRS, 2, D, M).transpose(2, 0, 1, 3)
    cols = np.stack([arr("L0_cond2_g_norm"), arr("L0_ffn_norm_w"), np.tile(arr("L0_cond2_q_scale"), 2),
                     np.tile(arr("L0_cond2_k_scale"), 2), np.tile(cond[0], 2)], 1)
    wkv = arr("L0_cond2_Wkv")
    pack_a = pack(PACK_A_AT, PACK_A_W, P, {
        "wt": arr("L0_cond_wt").T, "s_gate": arr("L0_cond_sw_gate"), "s_up": arr("L0_cond_sw_up"),
        "gate": pairs(arr("L0_cond_w_gate")), "up": pairs(arr("L0_cond_w_up")),
        "down": arr("L0_cond_w_down").reshape(PAIRS, P, D).transpose(1, 0, 2), "s_down": arr("L0_cond_sw_down")})
    pack_b = pack(PACK_B_AT, PACK_B_W, P, {
        "wqkv": arr("L0_attn_w_qkv"), "wproj": arr("L0_attn_w_proj"), "cols": cols, "wk": wkv[:, :CD],
        "wv": wkv[:, CD:], "router": arr("L0_ffn_router_w"),
        "rel_w1": arr("L0_cond2_w1"), "rel_w2": arr("L0_cond2_w2")})
    pack_c = pack(PACK_C_AT, PACK_C_W, G, {"cond": cond.T, "wg": arr("L0_cond_wg").T})
    rows = pack(ROW_AT, ROW_W, 1, {
        "b_proj": arr("L0_attn_b_proj"), "g_out": arr("L0_cond2_g_out"),
        "null_bias": arr("L0_cond2_null_attn_bias"), "w0": arr("L0_cond2_w0"), "b0": arr("L0_cond2_b0"),
        "g0": arr("L0_cond2_g0"), "b1": arr("L0_cond2_b1"), "g1": arr("L0_cond2_g1"), "b2": arr("L0_cond2_b2")})
    null_v = np.zeros((2, P), np.float32)
    null_v[0, :CD] = cond[1]
    null_v[1, CD:] = cond[1]
    w13 = np.concatenate([arr("L0_ffn_w1"), arr("L0_ffn_w3")], 2).transpose(1, 0, 2)
    w2 = arr("L0_ffn_w2").reshape(E, FC, P, D).transpose(2, 0, 1, 3).reshape(P, -1)
    arrays = {
        "x": arr("x").reshape(TOK, D), "pack_a": pack_a, "pack_b": pack_b, "pack_c": pack_c, "rows": rows,
        "null_v": null_v, "key_mask": arr("mask_BxS_bf1").view(np.uint8), "w_q": arr("L0_cond2_Wq"),
        "w_out": arr("L0_cond2_Wout").reshape(HP, P, D).transpose(1, 0, 2).reshape(P, -1),
        "w13": w13, "w2": w2, "consts": constants()}
    arrays = {k: np.ascontiguousarray(v) for k, v in arrays.items()}
    nc = _bacc.Bacc("TRN2", target_bir_lowering=False, num_devices=1)
    args = [nc.dram_tensor(f"in_{k}", v.shape, mybir.dt.from_np(v.dtype), kind="ExternalInput").ap()
            for k, v in arrays.items()]
    out = nc.dram_tensor("out_0", (TOK, D), F32, kind="ExternalOutput").ap()
    layer_kernel(nc, *args, out)
    r = _run(nc, [{f"in_{k}": v for k, v in arrays.items()}], core_ids=[0])
    return r.results[0]["out_0"].reshape(NSEQ, SEQ, D)
```
